# Optimizing a Trainium2 kernel written in Bass

```python
import numpy as np
import jax
import jax.numpy as jnp

def _softmax(x, axis=-1):
    return jax.nn.softmax(x, axis=axis)

def _gelu(x):
    return jax.nn.gelu(x, approximate=True)

def _silu(x):
    return jax.nn.silu(x)

def _sigmoid(x):
    return jax.nn.sigmoid(x)

def _layernorm(x, axis=-1, eps=1e-05):
    m = jnp.mean(x, axis=axis, keepdims=True)
    v = jnp.var(x, axis=axis, keepdims=True)
    return (x - m) / jnp.sqrt(v + eps)

def _scatter_add(tgt, idx, src, axis=0):
    return tgt.at[idx].add(src)

def _segment_sum(src, seg, n):
    return jax.ops.segment_sum(src, seg, n)
kernel_name = 'mk_adj_preln_d1_adj_r2_b2a7dd'

def setup_inputs(seed: int=0):
    np.random.seed(seed)
    _w = jnp.asarray

    def _rec_inputs():
        import jax
        import jax.numpy as jnp
        _gk = jax.random.key(seed)
        x = 7.22e-05 + 1 * jax.random.normal(jax.random.fold_in(_gk, 1), (4096, 512), jnp.float32)
        _a = jax.random.bernoulli(jax.random.fold_in(_gk, 2), 0.00195312, (4096, 4096))
        _a = jnp.logical_or(_a, jnp.swapaxes(_a, -1, -2))
        _a = jnp.logical_or(_a, jnp.eye(4096, dtype=bool))
        _af = _a.astype(jnp.float32)
        adj = _af
        return (x, adj)
    x, adj = _rec_inputs()

    def _L0_gnn_setup():
        import jax, jax.numpy as jnp
        import numpy as np
        N = 4096
        D = 512
        key = jax.random.key(seed)
        ks = jax.random.split(key, 13)
        w_scale = 1.0 / np.sqrt(D)
        inp = {'query': jax.random.normal(ks[0], (N, D), dtype=jnp.float32), 'key': jax.random.normal(ks[1], (N, D), dtype=jnp.float32), 'value': jax.random.normal(ks[2], (N, D), dtype=jnp.float32), 'adj_matrix': jax.random.randint(ks[3], (N, N), 0, 2).astype(jnp.float32), 'Wq': jax.random.normal(ks[4], (D, D), dtype=jnp.float32) * w_scale, 'bq': jax.random.normal(ks[5], (D,), dtype=jnp.float32) * 0.01, 'Wk': jax.random.normal(ks[6], (D, D), dtype=jnp.float32) * w_scale, 'bk': jax.random.normal(ks[7], (D,), dtype=jnp.float32) * 0.01, 'Wv': jax.random.normal(ks[8], (D, D), dtype=jnp.float32) * w_scale, 'bv': jax.random.normal(ks[9], (D,), dtype=jnp.float32) * 0.01, 'Wm': jax.random.normal(ks[10], (D, D), dtype=jnp.float32) * w_scale, 'bm': jax.random.normal(ks[11], (D,), dtype=jnp.float32) * 0.01}
        return inp
    _L0_gnn_all = _L0_gnn_setup()
    _L0_gnn_in = {k: v for k, v in _L0_gnn_all.items() if k in ('key', 'value', 'Wq', 'bq', 'Wk', 'bk', 'Wv', 'bv', 'Wm', 'bm')}
    del _L0_gnn_all
    return {'x': x, 'adj': adj, 'L0_gnn_key': _L0_gnn_in['key'], 'L0_gnn_value': _L0_gnn_in['value'], 'L0_gnn_Wq': _L0_gnn_in['Wq'], 'L0_gnn_bq': _L0_gnn_in['bq'], 'L0_gnn_Wk': _L0_gnn_in['Wk'], 'L0_gnn_bk': _L0_gnn_in['bk'], 'L0_gnn_Wv': _L0_gnn_in['Wv'], 'L0_gnn_bv': _L0_gnn_in['bv'], 'L0_gnn_Wm': _L0_gnn_in['Wm'], 'L0_gnn_bm': _L0_gnn_in['bm']}

def reference(x, adj, L0_gnn_key, L0_gnn_value, L0_gnn_Wq, L0_gnn_bq, L0_gnn_Wk, L0_gnn_bk, L0_gnn_Wv, L0_gnn_bv, L0_gnn_Wm, L0_gnn_bm):
    import jax
    import jax.numpy as jnp

    def _L0_gnn_ref(query, key, value, adj_matrix, Wq, bq, Wk, bk, Wv, bv, Wm, bm):
        import jax, jax.numpy as jnp
        import numpy as np
        N = 4096
        D = 512
        q = query @ Wq.T + bq
        k = key @ Wk.T + bk
        v = value @ Wv.T + bv
        scale = q.shape[0] ** 0.5
        scores = jnp.einsum('nd,md->nm', q, k) / scale
        adj_scores = scores * adj_matrix
        adj_scores = jnp.where(jnp.abs(adj_scores) < 1e-05, -1000000000.0, adj_scores)
        prob = jax.nn.softmax(adj_scores, axis=-1)
        x = jnp.einsum('nm,md->nd', prob, v)
        return x @ Wm.T + bm
    h = jnp.maximum(_layernorm(x, axis=-1), 0.0)
    x = x + _L0_gnn_ref(h, L0_gnn_key, L0_gnn_value, adj, L0_gnn_Wq, L0_gnn_bq, L0_gnn_Wk, L0_gnn_bk, L0_gnn_Wv, L0_gnn_bv, L0_gnn_Wm, L0_gnn_bm)
    return x

_drawn_inputs = setup_inputs


def setup_inputs(seed=0):
    import zlib

    import numpy as np

    out = dict(_drawn_inputs(seed))
    spreads = {}
    factors = {'L0_gnn_bq': 64.0, 'L0_gnn_bk': 64.0, 'L0_gnn_bv': 6.089, 'L0_gnn_bm': 5.69}
    for name, (base, spread) in spreads.items():
        noise = np.random.default_rng([zlib.crc32(name.encode()), seed]).standard_normal(out[name].shape)
        drawn = base * np.exp(spread * noise) if base else spread * noise
        out[name] = jnp.asarray(drawn.astype(out[name].dtype))
    for name, factor in factors.items():
        out[name] = (out[name] * factor).astype(out[name].dtype)
    return out
```

```python
import concourse.bass as bass
from concourse import mybir
from contextlib import ExitStack


def adjacency_attention(nc, x, adj, key, value, Wq, bq, Wk, bk, Wv, bv, Wm, bm, out):
    fp32 = mybir.dt.float32
    fp16 = mybir.dt.float16
    i32 = mybir.dt.int32
    ALU = mybir.AluOpType
    ACT = mybir.ActivationFunctionType
    X = mybir.AxisListType.X

    ABSMAX = bass.bass_isa.ReduceOp.absmax

    P = 128
    N, D = x.shape
    M = key.shape[0]
    ND = D // P
    CW = 512
    CM = CW // P
    NC = M // CW
    NB = N // P
    STEPS = NB * NC
    PASS = 2 * NC
    NPASS = STEPS // PASS
    LAG_T = 9
    LAG_V = 10
    NPAIR = NC // 2
    ADJ_SLOTS = 4
    EPS = 1e-5
    ROOT = float(N) ** 0.5
    TOP = 8192.0
    PSCALE = 16384.0
    EXPONENT = 0x7F800000
    assert ROOT == 64.0 and NC == 8 and N % (2 * P) == 0 and M % CW == 0 and D == 4 * P

    ctx = ExitStack()
    with ctx:
        def sb(name, shape, dt=fp32):
            return ctx.enter_context(nc.sbuf_tensor(name, shape, dt))

        def sem(name):
            return ctx.enter_context(nc.semaphore(name))

        Kbuf = sb("Kbuf", [P, NC * 2048])
        Vbuf = sb("Vbuf", [P, M // P * D])
        Zbuf = sb("Zbuf", [P, 2, NC * CW])
        adjb = sb("adjb", [P, ADJ_SLOTS, CW])
        A_sb = sb("A_sb", [P, ND, D])
        B_sb = sb("B_sb", [P, ND, D])
        xq = sb("xq", [P, D])
        ho = sb("ho", [P, ND, P])
        osb = sb("osb", [P, D])
        xr = sb("xr", [P, D])
        qT = sb("qT", [P, 2, 2, ND, P], fp16)
        pT = sb("pT", [P, 2, 2, CM, P], fp16)
        drop = sb("drop", [P, CW])
        qbias = sb("qbias", [P, D])
        obias = sb("obias", [P, D])
        ident = sb("ident", [P, P])
        bqc = sb("bqc", [P, ND])
        bkc = sb("bkc", [P, ND])
        bvc = sb("bvc", [P, ND])
        wcol = sb("wcol", [P, ND + 1])
        kmax = sb("kmax", [P, NC])
        vsum = sb("vsum", [P, NC + 2])
        kst = sb("kst", [P, 7])
        vst = sb("vst", [P, 7])
        bn = sb("bn", [P, 6])
        mv = sb("mv", [P, 2])
        rstd = sb("rstd", [P, 2])
        mhalf = sb("mhalf", [P, 1])
        eps = sb("eps", [P, 1])
        qst = sb("qst", [P, 4])
        rs = sb("rs", [P, 2, 4])
        unit = sb("unit", [P, 2])
        cmx = sb("cmx", [P, 2, NC])
        smx = sb("smx", [P, 2, 3])
        psums = sb("psums", [P, 2, NPAIR])
        rsum = sb("rsum", [P, 2])

        def bank(name):
            return ctx.enter_context(nc.psum_tensor(name, [P, 512], fp32))

        S = [bank("S0"), bank("S1")]
        T = [bank("T0"), bank("T1")]
        O = [bank("O0"), bank("O1")]
        M0, M1 = bank("M0"), bank("M1")

        z0, z1 = Zbuf[:, 0, :], Zbuf[:, 1, :]
        Wq_sb = z0[:, 0:2048].rearrange("p (k d) -> p k d", k=ND)
        Wk_sb = z0[:, 2048:4096].rearrange("p (k d) -> p k d", k=ND)
        bqrep = z1[:, 0:512].rearrange("p (k n) -> p k n", k=ND)
        bvrep = z1[:, 512:1024].rearrange("p (k n) -> p k n", k=ND)
        ones = z1[:, 1024:1152]
        bmrow = z1[0:1, 1152:1664]
        VW = M // P * D - 3 * 2048
        Wv_sb = Vbuf[:, VW:VW + 2048].rearrange("p (k d) -> p k d", k=ND)
        Wm_sb = Vbuf[:, VW + 2048:VW + 4096].rearrange("p (k d) -> p k d", k=ND)
        WmT = Vbuf[:, VW + 4096:VW + 6144].rearrange("p (k d) -> p k d", k=ND)
        V_CLEAR = 4
        assert (2 + CM * V_CLEAR) * D <= VW
        START = [S[0], S[1], T[0], T[1]]
        N_WEIGHT_BANKS = 3 * ND + 3
        V_FIRST = 2

        def k_stage(g):
            at = Kbuf[:, (g + 1) * 2048:(g + 2) * 2048] if g < NC - 1 else z1[:, 2048:4096]
            return at.rearrange("p (j d) -> p j d", j=CM)

        def k_pair(g, half, s):
            at = (g * 2 + half) * ND * CW + s * CW
            return Kbuf[:, :].bitcast(fp16)[:, at:at + CW]

        V_PARTS = [(g * CM, CM) for g in range(NC - 1)] + [(M // P - 4, 2), (M // P - 2, 1), (M // P - 1, 1)]

        def v_stage(j, n=1):
            if j >= M // P - 2:
                return (xr, osb)[j - (M // P - 2)][:, :]
            return Vbuf[:, (j + 2) * D:(j + 2 + n) * D]

        def v_pair(j, half):
            at = (2 * j + half) * D
            return Vbuf[:, :].bitcast(fp16)[:, at:at + D]

        def blk(ap, s):
            return ap[:, s * P:(s + 1) * P]

        w_in = [sem(f"w_in_{n}") for n in ("qk", "v", "m")]
        b_in = sem("b_in")
        k_in = [sem(f"k_in{g}") for g in range(NC)]
        v_in = [sem(f"v_in{g}") for g in range(len(V_PARTS))]
        x_in = sem("x_in")
        x2_in = sem("x2_in")
        adj_in = [sem(f"adj_in{s}") for s in range(ADJ_SLOTS)]
        stored = sem("stored")
        ident_ready = sem("ident_ready")
        reps_ready = sem("reps_ready")
        start_mm = sem("start_mm")
        start_free = sem("start_free")
        ones_ready = sem("ones_ready")
        kmax_ready = sem("kmax_ready")
        k_small = sem("k_small")
        k_all = sem("k_all")
        k_hi = sem("k_hi")
        v_small = sem("v_small")
        v_sum = sem("v_sum")
        v_all = sem("v_all")
        v_hi = sem("v_hi")
        v_ready = sem("v_ready")
        bn_ready = sem("bn_ready")
        stats_ready = sem("stats_ready")
        var_ready = sem("var_ready")
        rstd_ready = sem("rstd_ready")
        xn_ready = sem("xn_ready")
        xT_done = sem("xT_done")
        hT_ready = sem("hT_ready")
        qp_done = sem("qp_done")
        q_small = sem("q_small")
        q_scaled = sem("q_scaled")
        qTp_done = sem("qTp_done")
        q_hi = sem("q_hi")
        q_ready = sem("q_ready")
        scores_done = sem("scores_done")
        z1_ready = sem("z1_ready")
        abs_ready = sem("abs_ready")
        drop_ready = sem("drop_ready")
        cmax_ready = sem("cmax_ready")
        rowmax_ready = sem("rowmax_ready")
        smax_ready = sem("smax_ready")
        exp_done = sem("exp_done")
        pT_done = sem("pT_done")
        p_hi = sem("p_hi")
        p_lo = sem("p_lo")
        pv_done = sem("pv_done")
        rsum_ready = sem("rsum_ready")
        osb_ready = sem("osb_ready")
        oTp_done = sem("oTp_done")
        oT_ready = sem("oT_ready")
        outp_done = sem("outp_done")
        xr_ready = sem("xr_ready")
        res_ready = sem("res_ready")

        Q_SMALL = 8

        def wait(eng, s, v):
            if not (isinstance(v, int) and v <= 0):
                eng.wait_ge(s, v)

        class Step:

            def __init__(self, i, j):
                self.t, self.j, self.c, self.p = PASS * i + j, j, j % NC, (j // NC) % 2
                self.b = 2 * i + j // NC
                fixed = isinstance(i, int)
                t, b = (self.t, self.b) if fixed else (PASS + j, 2 + j // NC)
                late = fixed and i > 0
                self.has_scores = not late or t < STEPS
                self.has_max = t >= 1 and (not late or t - 1 < STEPS)
                self.has_T = t >= LAG_T and (not late or t - LAG_T < STEPS)
                self.has_V = t >= LAG_V and (not late or t - LAG_V < STEPS)
                self.has_prep = not late or b + 1 < NB
                self.has_exp = b >= 1 and (not late or b - 1 < NB)
                self.has_out = b >= 2 and (not late or b - 2 < NB)
                self.more_adj = not late or t + ADJ_SLOTS < STEPS
                self.more_x = not late or b + 2 < NB
                self.pair = NPAIR * 2 * i + (j - LAG_T) // 2
                self.adj_n = (PASS // ADJ_SLOTS) * i + j // ADJ_SLOTS

        LAST = LAG_V + 5
        FIRST = 2

        def run(engine, step):
            for i in range(FIRST):
                for j in range(PASS):
                    step(Step(i, j))
            with engine.Fori(FIRST, NPASS - 1) as i:
                for j in range(PASS):
                    step(Step(i, j))
            for j in range(PASS):
                step(Step(NPASS - 1, j))
            for j in range(LAST):
                step(Step(NPASS, j))

        block = ctx.enter_context(nc.Block())

        @block.sync
        def _(sp):
            def load_adj(b, c, slot):
                sp.dma_start(adjb[:, slot, :], adj[bass.ds(b * P, P), c * CW:(c + 1) * CW])\
                    .then_inc(adj_in[slot], 16)

            kv = key.rearrange("(g j p) d -> g p j d", p=P, j=CM)
            vv = value.rearrange("(j p) d -> p j d", p=P)
            sp.dma_start(Wq_sb, Wq.rearrange("(p k) d -> p k d", k=ND)).then_inc(w_in[0], 16)
            sp.dma_start(Wk_sb, Wk.rearrange("(p k) d -> p k d", k=ND)).then_inc(w_in[0], 16)
            sp.dma_start(xq[:, :], x[0:P, :]).then_inc(x_in, 16)
            for g in range(NC):
                sp.dma_start(k_stage(g), kv[g, :, :, :]).then_inc(k_in[g], 16)
            sp.dma_start(Wv_sb, Wv.rearrange("(p k) d -> p k d", k=ND)).then_inc(w_in[1], 16)
            sp.dma_start(Wm_sb, Wm.rearrange("(k p) d -> p k d", p=P)).then_inc(w_in[2], 16)
            for t in range(ADJ_SLOTS):
                load_adj(0, t, t)
            for g, (j, m) in enumerate(V_PARTS):
                if g == V_CLEAR:
                    sp.wait_ge(start_mm, N_WEIGHT_BANKS)
                sp.dma_start(v_stage(j, m).rearrange("p (j d) -> p j d", j=m), vv[:, j:j + m, :])\
                    .then_inc(v_in[g], 16)
            sp.wait_ge(qTp_done, 1)
            sp.dma_start(xq[:, :], x[P:2 * P, :]).then_inc(x_in, 16)

            def step(s):
                if s.has_scores and s.more_adj:
                    wait(sp, z1_ready, s.t + 1)
                    load_adj(s.b + (s.c + ADJ_SLOTS) // NC, (s.c + ADJ_SLOTS) % NC, s.j % ADJ_SLOTS)
                if s.c == 0 and s.has_out:
                    o = s.b - 2
                    wait(sp, stored, 16 * o)
                    sp.dma_start(xr[:, :], x[bass.ds(o * P, P), :]).then_inc(x2_in, 16)
                if s.c == 6 and s.more_x:
                    wait(sp, qTp_done, s.b + 2)
                    sp.dma_start(xq[:, :], x[bass.ds((s.b + 2) * P, P), :]).then_inc(x_in, 16)
                if s.c == 7 and s.has_out:
                    o = s.b - 2
                    wait(sp, res_ready, o + 1)
                    sp.dma_start(out[bass.ds(o * P, P), :], xr[:, :]).then_inc(stored, 16)

            run(sp, step)
            sp.wait_ge(res_ready, NB)
            sp.dma_start(out[(NB - 1) * P:NB * P, :], xr[:, :]).then_inc(stored, 16)
            sp.wait_ge(stored, 16 * NB)

        @block.gpsimd
        def _(pool):
            pool.memset(mhalf[:, :], -0.5)
            pool.memset(eps[:, :], EPS)
            pool.memset(ident[:, :], 0.0).then_inc(ident_ready, 1)
            pool.wait_ge(ident_ready, 1)
            pool.affine_select(out=ident[:, :], in_=ident[:, :], compare_op=ALU.not_equal, fill=1.0,
                               base=0, pattern=[[-1, P]], channel_multiplier=1).then_inc(ident_ready, 1)

            def rstd_of(n):
                wait(pool, stats_ready, n)
                nc.gpsimd.tensor_tensor(rstd[:, 0:1], mv[:, 1:2], eps[:, :], ALU.add).then_inc(var_ready, 1)
                wait(pool, var_ready, n)
                nc.gpsimd.tensor_tensor(rstd[:, 1:2], rstd[:, 0:1], mhalf[:, :], ALU.pow).then_inc(rstd_ready, 1)

            rstd_of(1)
            pool.wait_ge(k_small, 1)
            nc.gpsimd.partition_all_reduce(kst[:, 1:2], kst[:, 0:1], P, ABSMAX).then_inc(k_all, 1)
            pool.wait_ge(v_small, 1)
            nc.gpsimd.partition_all_reduce(vst[:, 1:2], vst[:, 0:1], P, ABSMAX).then_inc(v_all, 1)

            def step(s):
                if s.c == 0 and s.has_prep:
                    rstd_of(s.b + 2)
                if s.c == 2 and s.has_out:
                    wait(pool, x2_in, 16 * (s.b - 1))
                    nc.gpsimd.tensor_tensor(xr[:, :], xr[:, :], obias[:, :], ALU.add).then_inc(xr_ready, 1)

            run(pool, step)

        @block.tensor
        def _(pe):
            def split_product(ps, lhs, rhs, start, stop):
                nc.tensor.matmul(ps, lhs[0], rhs[0], start=start, stop=False)
                nc.tensor.matmul(ps, lhs[0], rhs[1], start=False, stop=False)
                return nc.tensor.matmul(ps, lhs[1], rhs[0], start=False, stop=stop)

            def transpose_x(n):
                wait(pe, xn_ready, n)
                wait(pe, q_ready, n - 1)
                for s in range(ND):
                    last = nc.tensor.transpose(blk(M0, s), blk(xq, s), ident[:, :])
                last.then_inc(xT_done, 1)

            def project_q(n, out_before):
                wait(pe, hT_ready, n)
                for s in range(ND):
                    nc.tensor.matmul(M0[:, 0:1], ho[:, s, :], wcol[:, s:s + 1], start=(s == 0), stop=(s == ND - 1))
                wait(pe, res_ready, out_before)
                for s in range(ND):
                    last = nc.tensor.matmul(M1[:, :], ho[:, s, :], A_sb[:, s, :], start=(s == 0), stop=(s == ND - 1))
                last.then_inc(qp_done, 1)

            def transpose_q(n):
                wait(pe, q_scaled, n)
                for s in range(ND):
                    last = nc.tensor.transpose(blk(M0, s), blk(xq, s), ident[:, :])
                last.then_inc(qTp_done, 1)

            def free(n):
                wait(pe, start_free, n - 3)

            pe.wait_ge(w_in[0], 32)
            n = 0
            for s in range(ND):
                free(n)
                for k in range(ND):
                    last = nc.tensor.matmul(START[n % 4][:, :], Wq_sb[:, k, s * P:(s + 1) * P], Wk_sb[:, k, :],
                                            start=(k == 0), stop=(k == ND - 1))
                last.then_inc(start_mm, 1)
                n += 1
            free(n)
            pe.wait_ge(reps_ready, 1)
            for k in range(ND):
                last = nc.tensor.matmul(START[n % 4][:, :], bqrep[:, k, :], Wk_sb[:, k, :], start=(k == 0), stop=(k == ND - 1))
            last.then_inc(start_mm, 1)
            n += 1
            free(n)
            for s in range(ND + 1):
                for k in range(ND):
                    lhs = Wq_sb[:, k, s * P:(s + 1) * P] if s < ND else bqrep[:, k, :]
                    last = nc.tensor.matmul(START[n % 4][:, s:s + 1], lhs, bkc[:, k:k + 1], start=(k == 0), stop=(k == ND - 1))
            last.then_inc(start_mm, 1)
            n += 1
            pe.wait_ge(ident_ready, 2)
            transpose_x(1)
            pe.wait_ge(start_free, ND + 2)
            project_q(1, 0)
            pe.wait_ge(w_in[2], 16)
            wmv = Wm_sb.rearrange("f s (e k) -> f s k e", k=ND)
            for k in range(ND):
                free(n)
                for s in range(ND):
                    last = nc.tensor.transpose(blk(START[n % 4], s), wmv[:, s, k, :], ident[:, :])
                last.then_inc(start_mm, 1)
                n += 1
            pe.wait_ge(w_in[1], 16)
            for s in range(ND):
                free(n)
                if s == 0:
                    pe.wait_ge(start_free, n)
                for k in range(ND):
                    last = nc.tensor.matmul(START[n % 4][:, :], Wv_sb[:, k, s * P:(s + 1) * P], WmT[:, k, :],
                                            start=(k == 0), stop=(k == ND - 1))
                last.then_inc(start_mm, 1)
                n += 1
            free(n)
            for k in range(ND):
                nc.tensor.matmul(START[n % 4][:, :], bvrep[:, k, :], WmT[:, k, :], start=(k == 0), stop=False)
            nc.tensor.matmul(START[n % 4][:, :], ones[0:1, :], bmrow, start=False, stop=True).then_inc(start_mm, 1)
            n += 1
            assert n == N_WEIGHT_BANKS
            for g in range(NC):
                pe.wait_ge(k_in[g], 16)
                for s in range(ND):
                    free(n)
                    for m in range(CM):
                        last = nc.tensor.transpose(blk(START[n % 4], m), k_stage(g)[:, m, s * P:(s + 1) * P], ident[:, :])
                    last.then_inc(start_mm, 1)
                    n += 1
            transpose_q(1)
            pe.wait_ge(start_free, n)

            def step(s):
                if s.has_scores:
                    if s.c == 0:
                        wait(pe, q_ready, s.b + 1)
                    wait(pe, z1_ready, s.t - 1)
                    for f in range(ND):
                        last = split_product(S[s.j % 2][:, :], [qT[:, s.p, h, f, :] for h in range(2)],
                                             [k_pair(s.c, h, f) for h in range(2)], f == 0, f == ND - 1)
                    last.then_inc(scores_done, 1)
                if s.has_T:
                    ju = s.j - LAG_T
                    if ju % 2 == 0:
                        wait(pe, exp_done, s.pair + 1)
                    wait(pe, p_lo, s.t - LAG_T - 1)
                    probs = Zbuf[:, (ju // NC) % 2, (ju % NC) * CW:(ju % NC + 1) * CW]
                    for m in range(CM):
                        last = nc.tensor.transpose(blk(T[ju % 2], m), blk(probs, m), ident[:, :])
                    last.then_inc(pT_done, 1)
                if s.has_V:
                    jw = s.j - LAG_V
                    wait(pe, p_lo, s.t - LAG_V + 1)
                    if jw % NC == 0:
                        wait(pe, osb_ready, s.b - 2)
                    if isinstance(s.t, int) and s.t < PASS:
                        wait(pe, v_ready, (jw + 1) * CM if s.t < PASS - 1 else M // P)
                    for m in range(CM):
                        tile = (jw % NC) * CM + m
                        last = split_product(O[(jw // NC) % 2][:, :], [pT[:, jw % 2, h, m, :] for h in range(2)],
                                             [v_pair(tile, h) for h in range(2)],
                                             jw % NC == 0 and m == 0, jw % NC == NC - 1 and m == CM - 1)
                    last.then_inc(pv_done, 1)
                if s.c == 2 and s.has_prep:
                    transpose_x(s.b + 2)
                if s.c == 3 and s.has_prep:
                    project_q(s.b + 2, s.b - 2)
                if s.c == 4 and s.has_out:
                    o = s.b - 2
                    wait(pe, osb_ready, o + 1)
                    if s.has_prep:
                        wait(pe, q_small, Q_SMALL * (s.b + 1) + 1)
                    wait(pe, res_ready, o)
                    for f in range(ND):
                        last = nc.tensor.transpose(blk(M1, f), blk(osb, f), ident[:, :])
                    last.then_inc(oTp_done, 1)
                if s.c == 5 and s.has_prep:
                    transpose_q(s.b + 2)
                if s.c == 6 and s.has_out:
                    wait(pe, oT_ready, s.b - 1)
                    for f in range(ND):
                        last = nc.tensor.matmul(M1[:, :], ho[:, f, :], B_sb[:, f, :], start=(f == 0), stop=(f == ND - 1))
                    last.then_inc(outp_done, 1)

            run(pe, step)

        @block.scalar
        def _(act):
            act.dma_start(bqc[:, :], bq.rearrange("(p k) -> p k", k=ND)).then_inc(b_in, 16)
            act.dma_start(bkc[:, :], bk.rearrange("(p k) -> p k", k=ND)).then_inc(b_in, 16)
            act.dma_start(bvc[:, :], bv.rearrange("(p k) -> p k", k=ND)).then_inc(b_in, 16)
            act.dma_start(bmrow, bm.rearrange("(a n) -> a n", a=1)).then_inc(b_in, 16)

            def h_T(n, out_before):
                wait(act, xT_done, n)
                wait(act, outp_done, out_before)
                nc.scalar.activation(ho[:, :, :].rearrange("p s n -> p (s n)"), M0[:, :], ACT.Relu).then_inc(hT_ready, 1)

            def q_high(n, p):
                wait(act, qTp_done, n)
                nc.scalar.activation(qT[:, p, 0, :, :].rearrange("p s n -> p (s n)"), M0[:, :], ACT.Copy).then_inc(q_hi, 1)

            n = 0

            def out_of(dst, width=512, scale=1.0):
                nonlocal n
                act.wait_ge(start_mm, n + 1)
                nc.scalar.activation(dst, START[n % 4][:, 0:width], ACT.Copy, scale=scale).then_inc(start_free, 1)
                n += 1

            for s in range(ND):
                out_of(A_sb[:, s, :])
            out_of(qbias[:, :])
            out_of(wcol[:, :], ND + 1, 1.0 / ROOT)
            h_T(1, 0)
            for k in range(ND):
                out_of(WmT[:, k, :])
            for s in range(ND):
                out_of(B_sb[:, s, :])
            out_of(obias[:, :])
            act.wait_ge(k_small, 5)
            for g in range(NC):
                for s in range(ND):
                    act.wait_ge(start_mm, n + 1)
                    nc.scalar.activation(k_pair(g, 0, s), START[n % 4][:, :], ACT.Copy,
                                         scale=kst[:, 4:5]).then_inc(k_hi, 1)
                    n += 1
            q_high(1, 0)
            for g, (j, m) in enumerate(V_PARTS):
                act.wait_ge(v_in[g], 16)
                if g > 0:
                    act.wait_ge(v_sum, g)
                scrap = pT[:, :, :, :, :].rearrange("p a b m n -> p (a b m n)")[:, 0:m * D]
                nc.scalar.activation(scrap, v_stage(j, m), ACT.Abs, scale=2.0 ** -14,
                                     accum_out=vsum[:, g:g + 1]).then_inc(v_sum, 1)

            def value_high(j):
                if j == 0:
                    act.wait_ge(v_small, 5)
                if j >= 2:
                    act.wait_ge(v_ready, j - 1)
                nc.scalar.activation(v_pair(j, 0), v_stage(j), ACT.Copy, scale=vst[:, 4:5]).then_inc(v_hi, 1)

            def step(s):
                if s.has_T:
                    ju = s.j - LAG_T
                    wait(act, pT_done, s.t - LAG_T + 1)
                    wait(act, pv_done, s.t - LAG_T - 1)
                    nc.scalar.activation(pT[:, ju % 2, 0, :, :].rearrange("p m n -> p (m n)"), T[ju % 2][:, :],
                                         ACT.Copy, scale=PSCALE).then_inc(p_hi, 1)
                if s.has_scores:
                    wait(act, z1_ready, s.t + 1)
                    wait(act, cmax_ready, s.t)
                    nc.scalar.activation(drop[:, :], Zbuf[:, s.p, s.c * CW:(s.c + 1) * CW], ACT.Abs).then_inc(abs_ready, 1)
                if s.c % 2 == 0 and s.has_exp:
                    k, pp = s.c // 2, 1 - s.p
                    if k == 0:
                        wait(act, smax_ready, 2 * s.b)
                    at = Zbuf[:, pp, 2 * k * CW:2 * (k + 1) * CW]
                    nc.scalar.activation(at, at, ACT.Exp, bias=smx[:, pp, 1:2], scale=smx[:, pp, 2:3],
                                         accum_out=psums[:, pp, k:k + 1]).then_inc(exp_done, 1)
                if isinstance(s.t, int) and V_FIRST <= s.t < V_FIRST + NC:
                    for j in range((s.t - V_FIRST) * CM, (s.t - V_FIRST + 1) * CM):
                        value_high(j)
                if s.c == 2 and s.has_prep:
                    h_T(s.b + 2, s.b - 2)
                if s.c == 4 and s.has_out:
                    wait(act, oTp_done, s.b - 1)
                    if s.has_prep:
                        wait(act, qp_done, s.b + 2)
                    nc.scalar.activation(ho[:, :, :].rearrange("p s n -> p (s n)"), M1[:, :], ACT.Copy).then_inc(oT_ready, 1)
                if s.c == 5 and s.has_prep:
                    q_high(s.b + 2, 1 - s.p)

            run(act, step)

        @block.vector
        def _(dve):
            def row_stats(n):
                wait(dve, x_in, 16 * n)
                nc.vector.bn_stats(bn[:, :], xq[:, :]).then_inc(bn_ready, 1)

            def mean_var():
                nc.vector.bn_aggr(mv[:, :], bn[:, :]).then_inc(stats_ready, 1)

            def normalise(n):
                wait(dve, rstd_ready, n)
                nc.vector.tensor_scalar(xq[:, :], xq[:, :], mv[:, 0:1], rstd[:, 1:2], ALU.subtract, ALU.mult)\
                    .then_inc(xn_ready, 1)

            def row_scales(n, p):
                first = Q_SMALL * (n - 1)
                wait(dve, qp_done, n)
                nc.vector.tensor_tensor(xq[:, :], M1[:, :], qbias[:, :], ALU.add).then_inc(q_small, 1)
                wait(dve, q_small, first + 1)
                nc.vector.tensor_reduce(qst[:, 0:1], xq[:, :], X, ALU.max, apply_absolute_value=True).then_inc(q_small, 1)
                wait(dve, q_small, first + 2)
                nc.vector.tensor_scalar_max(qst[:, 1:2], qst[:, 0:1], 2.0 ** -20).then_inc(q_small, 1)
                wait(dve, q_small, first + 3)
                nc.vector.tensor_scalar(qst[:, 2:3].bitcast(i32), qst[:, 1:2].bitcast(i32), EXPONENT, None,
                                        ALU.bitwise_and).then_inc(q_small, 1)
                wait(dve, q_small, first + 4)
                nc.vector.reciprocal(qst[:, 3:4], qst[:, 2:3]).then_inc(q_small, 1)
                nc.vector.tensor_scalar(unit[:, p:p + 1], qst[:, 2:3], kunit, None, ALU.mult).then_inc(q_small, 1)
                wait(dve, q_small, first + 5)
                nc.vector.tensor_scalar(rs[:, p, 0:1], qst[:, 3:4], kper, None, ALU.mult).then_inc(q_small, 1)
                wait(dve, q_small, first + 7)
                nc.vector.tensor_scalar(rs[:, p, 3:4], M0[:, 0:1], wcol[:, ND:ND + 1], rs[:, p, 0:1], ALU.add, ALU.mult)
                nc.vector.tensor_scalar(rs[:, p, 1:2], rs[:, p, 0:1], 1e-5, None, ALU.mult)
                nc.vector.tensor_scalar(rs[:, p, 2:3], rs[:, p, 0:1], -1e9, None, ALU.mult).then_inc(q_small, 1)
                nc.vector.tensor_scalar(xq[:, :], xq[:, :], qst[:, 3:4], TOP, ALU.mult, ALU.mult).then_inc(q_scaled, 1)

            def q_low(n, p):
                wait(dve, q_hi, n)
                nc.vector.tensor_tensor(qT[:, p, 1, :, :].rearrange("p s n -> p (s n)"), M0[:, :],
                                        qT[:, p, 0, :, :].rearrange("p s n -> p (s n)"), ALU.subtract).then_inc(q_ready, 1)

            kscale, kunit, kper = kst[:, 4:5], kst[:, 5:6], kst[:, 6:7]
            vscale, vunit = vst[:, 4:5], vst[:, 5:6]

            dve.wait_ge(b_in, 64)
            nc.vector.memset(ones, 1.0).then_inc(ones_ready, 1)
            dve.wait_ge(ones_ready, 1)
            for k in range(ND):
                nc.vector.tensor_scalar(bqrep[:, k, :], ones, bqc[:, k:k + 1], None, ALU.mult)
                last = nc.vector.tensor_scalar(bvrep[:, k, :], ones, bvc[:, k:k + 1], None, ALU.mult)
            last.then_inc(reps_ready, 1)
            row_stats(1)
            dve.wait_ge(bn_ready, 1)
            mean_var()
            normalise(1)

            def scale_of(st, chain, reduced, least, top, unit_of):
                dve.wait_ge(reduced, 1)
                nc.vector.tensor_scalar_max(st[:, 0:1], st[:, 1:2], least).then_inc(chain, 1)
                dve.wait_ge(chain, 2)
                nc.vector.tensor_scalar(st[:, 2:3].bitcast(i32), st[:, 0:1].bitcast(i32), EXPONENT, None,
                                        ALU.bitwise_and).then_inc(chain, 1)
                dve.wait_ge(chain, 3)
                nc.vector.reciprocal(st[:, 3:4], st[:, 2:3]).then_inc(chain, 1)
                nc.vector.tensor_scalar(st[:, 5:6], st[:, 2:3], unit_of, None, ALU.mult)
                dve.wait_ge(chain, 4)
                nc.vector.tensor_scalar(st[:, 4:5], st[:, 3:4], top, None, ALU.mult)
                nc.vector.tensor_scalar(st[:, 6:7], st[:, 3:4], 1.0 / unit_of, None, ALU.mult).then_inc(chain, 1)

            for g in range(NC):
                dve.wait_ge(k_in[g], 16)
                last = nc.vector.tensor_reduce(kmax[:, g:g + 1], k_stage(g).rearrange("p j d -> p (j d)"), X, ALU.max,
                                               apply_absolute_value=True)
            last.then_inc(kmax_ready, 1)
            dve.wait_ge(kmax_ready, 1)
            nc.vector.tensor_reduce(kst[:, 0:1], kmax[:, :], X, ALU.max).then_inc(k_small, 1)
            scale_of(kst, k_small, k_all, 2.0 ** -40, TOP, 1.0 / (TOP * TOP * ROOT))
            dve.wait_ge(k_small, 5)
            row_scales(1, 0)
            n = N_WEIGHT_BANKS
            for g in range(NC):
                for s in range(ND):
                    dve.wait_ge(k_hi, g * ND + s + 1)
                    nc.vector.scalar_tensor_tensor(out=k_pair(g, 1, s), in0=START[n % 4][:, :], scalar=kscale,
                                                   in1=k_pair(g, 0, s), op0=ALU.mult, op1=ALU.subtract)\
                        .then_inc(start_free, 1)
                    n += 1
            q_low(1, 0)

            def value_low(j):
                dve.wait_ge(v_hi, j + 1)
                nc.vector.scalar_tensor_tensor(out=v_pair(j, 1), in0=v_stage(j), scalar=vscale,
                                               in1=v_pair(j, 0), op0=ALU.mult, op1=ALU.subtract).then_inc(v_ready, 1)

            def step(s):
                r = s.p
                z = Zbuf[:, r, s.c * CW:(s.c + 1) * CW]
                if s.c == 0 and s.has_prep:
                    row_stats(s.b + 2)
                if s.has_scores:
                    if s.c == 0:
                        wait(dve, q_small, Q_SMALL * (s.b + 1))
                        if s.has_prep:
                            wait(dve, bn_ready, s.b + 2)
                    wait(dve, scores_done, s.t + 1)
                    wait(dve, adj_in[s.j % ADJ_SLOTS], 16 * (s.adj_n + 1))
                    wait(dve, pT_done, s.t - PASS + 1)
                    wait(dve, drop_ready, s.t)
                    nc.vector.scalar_tensor_tensor(out=z, in0=S[s.j % 2][:, :], scalar=rs[:, r, 3:4],
                                                   in1=adjb[:, s.j % ADJ_SLOTS, :], op0=ALU.add, op1=ALU.mult)\
                        .then_inc(z1_ready, 1)
                if s.c == 0 and s.has_prep:
                    mean_var()
                if s.has_max:
                    if not s.has_scores:
                        wait(dve, drop_ready, s.t)
                    q, c = (s.j - 1) // NC % 2, (s.j - 1) % NC
                    last = Zbuf[:, q, c * CW:(c + 1) * CW]
                    nc.vector.tensor_tensor_reduce(out=last, in0=drop[:, :], in1=last, scale=1.0, scalar=-3.4e38,
                                                   op0=ALU.add, op1=ALU.max, accum_out=cmx[:, q, c:c + 1])\
                        .then_inc(cmax_ready, 1)
                    if s.c == 0:
                        wait(dve, cmax_ready, s.t)
                        nc.vector.tensor_reduce(smx[:, q, 0:1], cmx[:, q, :], X, ALU.max).then_inc(rowmax_ready, 1)
                        wait(dve, exp_done, NPAIR * (s.b - 2))
                        nc.vector.tensor_copy(smx[:, q, 2:3], unit[:, q:q + 1]).then_inc(smax_ready, 1)
                        wait(dve, rowmax_ready, s.b)
                        nc.vector.tensor_scalar(smx[:, q, 1:2], smx[:, q, 0:1], unit[:, q:q + 1], -1.0,
                                                ALU.mult, ALU.mult).then_inc(smax_ready, 1)
                if s.has_T:
                    ju = s.j - LAG_T
                    wait(dve, p_hi, s.t - LAG_T + 1)
                    nc.vector.scalar_tensor_tensor(out=pT[:, ju % 2, 1, :, :].rearrange("p m n -> p (m n)"),
                                                   in0=T[ju % 2][:, :], scalar=PSCALE,
                                                   in1=pT[:, ju % 2, 0, :, :].rearrange("p m n -> p (m n)"),
                                                   op0=ALU.mult, op1=ALU.subtract).then_inc(p_lo, 1)
                if s.has_scores:
                    wait(dve, abs_ready, s.t + 1)
                    nc.vector.tensor_scalar(drop[:, :], drop[:, :], rs[:, r, 1:2], rs[:, r, 2:3], ALU.is_lt, ALU.mult)\
                        .then_inc(drop_ready, 1)
                if isinstance(s.t, int):
                    if s.t == V_FIRST - 1:
                        dve.wait_ge(v_sum, len(V_PARTS))
                        nc.vector.tensor_reduce(vst[:, 0:1], vsum[:, :], X, ALU.add).then_inc(v_small, 1)
                        scale_of(vst, v_small, v_all, 2.0 ** -40, 1.0, 1.0 / PSCALE)
                    if V_FIRST <= s.t < V_FIRST + NC:
                        for j in range((s.t - V_FIRST) * CM, (s.t - V_FIRST + 1) * CM):
                            value_low(j)
                if s.c == 1 and s.has_prep:
                    normalise(s.b + 2)
                if s.c == 1 and s.has_out:
                    o, q = s.b - 2, s.p
                    wait(dve, exp_done, NPAIR * (o + 1))
                    nc.vector.tensor_reduce(rsum[:, 0:1], psums[:, q, :], X, ALU.add).then_inc(rsum_ready, 1)
                    wait(dve, rsum_ready, 2 * o + 1)
                    nc.vector.reciprocal(rsum[:, 1:2], rsum[:, 0:1]).then_inc(rsum_ready, 1)
                    wait(dve, rsum_ready, 2 * o + 2)
                    wait(dve, pv_done, NC * (o + 1))
                    wait(dve, oTp_done, o)
                    nc.vector.tensor_scalar(osb[:, :], O[q][:, :], rsum[:, 1:2], vunit, ALU.mult, ALU.mult)\
                        .then_inc(osb_ready, 1)
                if s.c == 3 and s.has_prep:
                    row_scales(s.b + 2, 1 - s.p)
                if s.c == 5 and s.has_prep:
                    q_low(s.b + 2, 1 - s.p)
                if s.c == 6 and s.has_out:
                    wait(dve, outp_done, s.b - 1)
                    wait(dve, xr_ready, s.b - 1)
                    nc.vector.tensor_tensor(xr[:, :], M1[:, :], xr[:, :], ALU.add).then_inc(res_ready, 1)

            run(dve, step)


_INS = ["x", "adj", "L0_gnn_key", "L0_gnn_value", "L0_gnn_Wq", "L0_gnn_bq", "L0_gnn_Wk", "L0_gnn_bk",
        "L0_gnn_Wv", "L0_gnn_bv", "L0_gnn_Wm", "L0_gnn_bm"]
_OUTS = [((4096, 512), "float32")]


def kernel(**inputs):
    import numpy as _np
    import concourse.bacc as _bacc
    from concourse import mybir as _mybir
    from concourse.bass_utils import run_bass_kernel_spmd as _run

    nc = _bacc.Bacc("TRN2", target_bir_lowering=False, num_devices=1)
    arrays, args = {}, []
    for name in _INS:
        a = _np.ascontiguousarray(inputs[name])
        arrays[f"in_{name}_dram"] = a
        args.append(nc.dram_tensor(f"in_{name}_dram", a.shape, _mybir.dt.from_np(a.dtype), kind="ExternalInput").ap())
    for i, (shape, dtype) in enumerate(_OUTS):
        dt = _mybir.dt.from_np(_np.dtype(dtype))
        args.append(nc.dram_tensor(f"out_{i}_dram", shape, dt, kind="ExternalOutput").ap())
    adjacency_attention(nc, *args)
    r = _run(nc, [arrays], core_ids=[0])
    return r.results[0]["out_0_dram"]
```

```python
import concourse.bass as bass
from concourse import mybir
from contextlib import ExitStack


def adjacency_attention(nc, x, adj, key, value, Wq, bq, Wk, bk, Wv, bv, Wm, bm, out):
    fp32 = mybir.dt.float32
    fp16 = mybir.dt.float16
    bf16 = mybir.dt.bfloat16
    i32 = mybir.dt.int32
    ALU = mybir.AluOpType
    ACT = mybir.ActivationFunctionType
    X = mybir.AxisListType.X

    ABSMAX = bass.bass_isa.ReduceOp.absmax

    P = 128
    N, D = x.shape
    M = key.shape[0]
    ND = D // P
    CW = 512
    CM = CW // P
    NC = M // CW
    NB = N // P
    STEPS = NB * NC
    PASS = 2 * NC
    NPASS = STEPS // PASS
    LAG_T = 9
    LAG_V = 10
    NPAIR = NC // 2
    ADJ_SLOTS = 4
    EPS = 1e-5
    ROOT = float(N) ** 0.5
    TOP = 8192.0
    PSCALE = 16384.0
    EXPONENT = 0x7F800000
    assert ROOT == 64.0 and NC == 8 and N % (2 * P) == 0 and M % CW == 0 and D == 4 * P

    ctx = ExitStack()
    with ctx:
        def sb(name, shape, dt=fp32):
            return ctx.enter_context(nc.sbuf_tensor(name, shape, dt))

        def sem(name):
            return ctx.enter_context(nc.semaphore(name))

        Kbuf = sb("Kbuf", [P, NC * 2048])
        Vbuf = sb("Vbuf", [P, M // P * D])
        Zbuf = sb("Zbuf", [P, 2, NC * CW])
        adjb = sb("adjb", [P, ADJ_SLOTS, CW])
        A_sb = sb("A_sb", [P, 2, ND, D], fp16)
        B_sb = sb("B_sb", [P, 2, ND, D], fp16)
        xq = sb("xq", [P, D])
        ho = sb("ho", [P, 2, ND, P], fp16)
        osb = sb("osb", [P, D])
        xr = sb("xr", [P, D])
        qT = sb("qT", [P, 2, 2, ND, P], fp16)
        pT = sb("pT", [P, 2, 2, CM, P], fp16)
        drop = sb("drop", [P, CW])
        qbias = sb("qbias", [P, D])
        obias = sb("obias", [P, D])
        ident = sb("ident", [P, P])
        bqc = sb("bqc", [P, ND])
        bkc = sb("bkc", [P, ND])
        bvc = sb("bvc", [P, ND])
        wcol = sb("wcol", [P, ND + 1])
        wpair = sb("wpair", [P, ND, 2], fp16)
        ksum = sb("ksum", [P, NC])
        vsum = sb("vsum", [P, NC + 2])
        wmax = sb("wmax", [P, 2, 4])
        ast, bst, wst = sb("ast", [P, 7]), sb("bst", [P, 7]), sb("wst", [P, 7])
        kst, vst = sb("kst", [P, 7]), sb("vst", [P, 7])
        ounit = sb("ounit", [P, 1])
        bn = sb("bn", [P, 6])
        mv = sb("mv", [P, 2])
        rstd = sb("rstd", [P, 3])
        mhalf, half = sb("mhalf", [P, 1]), sb("half", [P, 1])
        hscale = sb("hscale", [P, 1])
        eps = sb("eps", [P, 1])
        qst = sb("qst", [P, 6])
        rs = sb("rs", [P, 2, 4])
        unit = sb("unit", [P, 2])
        cmx = sb("cmx", [P, 2, NC])
        smx = sb("smx", [P, 2, 3])
        psums = sb("psums", [P, 2, NPAIR])
        rsum = sb("rsum", [P, 2])

        def bank(name):
            return ctx.enter_context(nc.psum_tensor(name, [P, 512], fp32))

        S = [bank("S0"), bank("S1")]
        T = [bank("T0"), bank("T1")]
        O = [bank("O0"), bank("O1")]
        M0, M1 = bank("M0"), bank("M1")

        z0, z1 = Zbuf[:, 0, :], Zbuf[:, 1, :]

        def weight(z, at):
            return z[:, at:at + ND * D].rearrange("p (k d) -> p k d", k=ND)

        Wq_sb, Wk_sb = weight(z0, 0), weight(z0, ND * D)
        Wv_sb = weight(z1, 0)
        Wm_sb = weight(B_sb[:, :, :, :].rearrange("p a k d -> p (a k d)").bitcast(fp32), 0)
        WmT = weight(z0, ND * D)
        bqrep = pT[:, :, :, :, :].rearrange("p a b m n -> p (a b m n)").bitcast(fp32)[:, 0:ND * P]\
            .rearrange("p (k n) -> p k n", k=ND)
        bvrep = osb[:, :].rearrange("p (k n) -> p k n", k=ND)
        START = [T[0], T[1], O[0], O[1]]
        FILLS = ["A"] * ND + ["Wm^T"] * ND + ["B"] * (ND - 1) + [0] * ND + ["B"] + [1] * ND + ["bias"]
        FIRST_KEYS = 2
        for g in range(FIRST_KEYS, NC):
            FILLS += [g] * ND

        def last_fill(what):
            return max(n for n, f in enumerate(FILLS) if f == what)

        ASIDE = {last_fill("B"): S[0], last_fill("bias"): S[1]}

        def bank_of(n):
            return ASIDE[n] if n in ASIDE else START[sum(k not in ASIDE for k in range(n)) % len(START)]

        def last_in_bank(n):
            return max((k for k in range(n) if bank_of(k) is bank_of(n)), default=None)

        def read_by_act(n):
            return FILLS[n] == "Wm^T"

        def reads(n, by_act):
            return sum(read_by_act(k) == by_act for k in range(n + 1))

        ACT_SQUARES = [4, 5, 6, 6]
        V_SQUARES = [1, 2, 3, 4, 5, 6, 8, 10]
        V_TILES = [0] * 8 + [4 * n for n in range(9)]
        V_FIRST = V_TILES.count(0) - 1
        HS = 512.0

        def k_stage(g):
            at = Kbuf[:, (g + 1) * 2048:(g + 2) * 2048] if g < NC - 1 else z1[:, 2048:4096]
            return at.rearrange("p (j d) -> p j d", j=CM)

        def k_pair(g, half, s):
            at = (g * 2 + half) * ND * CW + s * CW
            return Kbuf[:, :].bitcast(fp16)[:, at:at + CW]

        V_PARTS = [(g * CM, CM) for g in range(NC - 1)] + [(M // P - 4, 2), (M // P - 2, 1), (M // P - 1, 1)]

        def v_stage(j, n=1):
            if j >= M // P - 2:
                return (xr, osb)[j - (M // P - 2)][:, :]
            return Vbuf[:, (j + 2) * D:(j + 2 + n) * D]

        def v_pair(j, half):
            at = (2 * j + half) * D
            return Vbuf[:, :].bitcast(fp16)[:, at:at + D]

        def blk(ap, s):
            return ap[:, s * P:(s + 1) * P]

        w_in = [sem(f"w_in{k}") for k in range(ND)]
        m_in, wv_in, bm_in = sem("m_in"), sem("wv_in"), sem("bm_in")
        b_in = sem("b_in")
        k_in = [sem(f"k_in{g}") for g in range(NC)]
        v_in = [sem(f"v_in{g}") for g in range(len(V_PARTS))]
        x_in = sem("x_in")
        x2_in = sem("x2_in")
        adj_in = [sem(f"adj_in{s}") for s in range(ADJ_SLOTS)]
        stored = sem("stored")
        ident_ready = sem("ident_ready")
        reps_ready = sem("reps_ready")
        start_mm = sem("start_mm")
        start_act = sem("start_act")
        start_dve = sem("start_dve")
        start_hi = sem("start_hi")
        aside_mm = sem("aside_mm")
        aside_read = sem("aside_read")
        wmax_ready = sem("wmax_ready")
        wmax_all = sem("wmax_all")
        a_small, b_small, w_small = sem("a_small"), sem("b_small"), sem("w_small")
        w_all = sem("w_all")
        w_hi = sem("w_hi")
        w_ready = sem("w_ready")
        k_sum = sem("k_sum")
        k_sum2 = sem("k_sum2")
        k_root = sem("k_root")
        k_small = sem("k_small")
        k_all = sem("k_all")
        v_small = sem("v_small")
        v_sum = sem("v_sum")
        v_all = sem("v_all")
        v_root = sem("v_root")
        ounit_ready = sem("ounit_ready")
        v_hi = sem("v_hi")
        v_ready = sem("v_ready")
        v_scaled = sem("v_scaled")
        v_ready2 = sem("v_ready2")
        bn_ready = sem("bn_ready")
        stats_ready = sem("stats_ready")
        var_ready = sem("var_ready")
        root_ready = sem("root_ready")
        rstd_ready = sem("rstd_ready")
        h_hi = sem("h_hi")
        oT_hi = sem("oT_hi")
        xn_ready = sem("xn_ready")
        xT_done = sem("xT_done")
        hT_ready = sem("hT_ready")
        qp_done = sem("qp_done")
        q_small = sem("q_small")
        q_scaled = sem("q_scaled")
        qTp_done = sem("qTp_done")
        q_hi = sem("q_hi")
        q_ready = sem("q_ready")
        scores_done = sem("scores_done")
        z1_ready = sem("z1_ready")
        abs_ready = sem("abs_ready")
        drop_ready = sem("drop_ready")
        cmax_ready = sem("cmax_ready")
        rowmax_ready = sem("rowmax_ready")
        smax_ready = sem("smax_ready")
        exp_done = sem("exp_done")
        pT_done = sem("pT_done")
        p_hi = sem("p_hi")
        p_lo = sem("p_lo")
        pv_done = sem("pv_done")
        rsum_ready = sem("rsum_ready")
        osb_ready = sem("osb_ready")
        oTp_done = sem("oTp_done")
        oT_ready = sem("oT_ready")
        outp_done = sem("outp_done")
        xr_ready = sem("xr_ready")
        res_ready = sem("res_ready")

        Q_SMALL = 10

        def wait(eng, s, v):
            if not (isinstance(v, int) and v <= 0):
                eng.wait_ge(s, v)

        class Step:

            def __init__(self, i, j):
                self.t, self.j, self.c, self.p = PASS * i + j, j, j % NC, (j // NC) % 2
                self.b = 2 * i + j // NC
                fixed = isinstance(i, int)
                t, b = (self.t, self.b) if fixed else (PASS + j, 2 + j // NC)
                late = fixed and i > 0
                self.has_scores = not late or t < STEPS
                self.has_max = t >= 1 and (not late or t - 1 < STEPS)
                self.has_T = t >= LAG_T and (not late or t - LAG_T < STEPS)
                self.has_V = t >= LAG_V and (not late or t - LAG_V < STEPS)
                self.has_prep = not late or b + 1 < NB
                self.has_exp = b >= 1 and (not late or b - 1 < NB)
                self.has_out = b >= 2 and (not late or b - 2 < NB)
                self.more_adj = not late or t + ADJ_SLOTS < STEPS
                self.more_x = not late or b + 2 < NB
                self.pair = NPAIR * 2 * i + (j - LAG_T) // 2
                self.adj_n = (PASS // ADJ_SLOTS) * i + j // ADJ_SLOTS

        def by_pool(j):
            return j % 4 == 3 and j > 3

        def in_pairs(eng, j):
            n = sum(by_pool(k) == by_pool(j) for k in range(j + 1))
            eng.wait_ge(v_ready2 if by_pool(j) else v_ready, n)

        LAST = LAG_V + 5
        FIRST = 2

        def run(engine, step):
            for i in range(FIRST):
                for j in range(PASS):
                    step(Step(i, j))
            with engine.Fori(FIRST, NPASS - 1) as i:
                for j in range(PASS):
                    step(Step(i, j))
            for j in range(PASS):
                step(Step(NPASS - 1, j))
            for j in range(LAST):
                step(Step(NPASS, j))

        block = ctx.enter_context(nc.Block())

        @block.sync
        def _(sp):
            def load_adj(b, c, slot):
                sp.dma_start(adjb[:, slot, :], adj[bass.ds(b * P, P), c * CW:(c + 1) * CW])\
                    .then_inc(adj_in[slot], 16)

            kv = key.rearrange("(g j p) d -> g p j d", p=P, j=CM)
            vv = value.rearrange("(j p) d -> p j d", p=P)
            wqv, wkv = [w.rearrange("(p k) d -> p k d", k=ND) for w in (Wq, Wk)]
            for k in range(ND):
                sp.dma_start(Wq_sb[:, k, :], wqv[:, k, :]).then_inc(w_in[k], 16)
                sp.dma_start(Wk_sb[:, k, :], wkv[:, k, :]).then_inc(w_in[k], 16)
            sp.dma_start(xq[:, :], x[0:P, :]).then_inc(x_in, 16)
            sp.dma_start(Wm_sb, Wm.rearrange("(k p) d -> p k d", p=P)).then_inc(m_in, 16)
            sp.dma_start(Wv_sb, Wv.rearrange("(p k) d -> p k d", k=ND)).then_inc(wv_in, 16)
            for g in range(NC):
                sp.dma_start(k_stage(g), kv[g, :, :, :]).then_inc(k_in[g], 16)
            for t in range(ADJ_SLOTS):
                load_adj(0, t, t)
            for g, (j, m) in enumerate(V_PARTS):
                if g == 4:
                    sp.wait_ge(qTp_done, 1)
                    sp.dma_start(xq[:, :], x[P:2 * P, :]).then_inc(x_in, 16)
                if g == len(V_PARTS) - 1:
                    sp.wait_ge(start_mm, last_fill("bias") + 1)
                sp.dma_start(v_stage(j, m).rearrange("p (j d) -> p j d", j=m), vv[:, j:j + m, :])\
                    .then_inc(v_in[g], 16)

            def step(s):
                if s.has_scores and s.more_adj:
                    wait(sp, z1_ready, s.t + 1)
                    load_adj(s.b + (s.c + ADJ_SLOTS) // NC, (s.c + ADJ_SLOTS) % NC, s.j % ADJ_SLOTS)
                if s.c == 0 and s.has_out:
                    o = s.b - 2
                    wait(sp, stored, 16 * o)
                    sp.dma_start(xr[:, :], x[bass.ds(o * P, P), :]).then_inc(x2_in, 16)
                if s.c == 6 and s.more_x:
                    wait(sp, qTp_done, s.b + 2)
                    sp.dma_start(xq[:, :], x[bass.ds((s.b + 2) * P, P), :]).then_inc(x_in, 16)
                if s.c == 7 and s.has_out:
                    o = s.b - 2
                    wait(sp, res_ready, o + 1)
                    sp.dma_start(out[bass.ds(o * P, P), :], xr[:, :]).then_inc(stored, 16)

            run(sp, step)
            sp.wait_ge(res_ready, NB)
            sp.dma_start(out[(NB - 1) * P:NB * P, :], xr[:, :]).then_inc(stored, 16)
            sp.wait_ge(stored, 16 * NB)

        @block.gpsimd
        def _(pool):
            pool.memset(mhalf[:, :], -0.5)
            pool.memset(half[:, :], 0.5)
            pool.memset(hscale[:, :], HS)
            pool.memset(eps[:, :], EPS)
            pool.memset(ident[:, :], 0.0).then_inc(ident_ready, 1)
            pool.wait_ge(ident_ready, 1)
            pool.affine_select(out=ident[:, :], in_=ident[:, :], compare_op=ALU.not_equal, fill=1.0,
                               base=0, pattern=[[-1, P]], channel_multiplier=1).then_inc(ident_ready, 1)

            def rstd_of(n):
                wait(pool, stats_ready, n)
                nc.gpsimd.tensor_tensor(rstd[:, 0:1], mv[:, 1:2], eps[:, :], ALU.add).then_inc(var_ready, 1)
                wait(pool, var_ready, n)
                nc.gpsimd.tensor_tensor(rstd[:, 1:2], rstd[:, 0:1], mhalf[:, :], ALU.pow).then_inc(root_ready, 1)
                wait(pool, root_ready, n)
                nc.gpsimd.tensor_tensor(rstd[:, 2:3], rstd[:, 1:2], hscale[:, :], ALU.mult).then_inc(rstd_ready, 1)

            rstd_of(1)

            def over_rows(dst, src, ready, done):
                wait(pool, *ready)
                nc.gpsimd.partition_all_reduce(dst, src, P, ABSMAX).then_inc(done, 1)

            over_rows(wmax[:, 1, 0:2], wmax[:, 0, 0:2], (wmax_ready, 1), wmax_all)
            over_rows(wst[:, 1:2], wst[:, 0:1], (w_small, 1), w_all)
            over_rows(wmax[:, 1, 2:4], wmax[:, 0, 2:4], (wmax_ready, 2), wmax_all)
            over_rows(kst[:, 2:3], kst[:, 0:1], (k_small, 1), k_root)
            pool.wait_ge(k_root, 1)
            nc.gpsimd.tensor_tensor(kst[:, 1:2], kst[:, 2:3], half[:, :], ALU.pow).then_inc(k_all, 1)

            def step(s):
                if s.c == 0 and s.has_prep:
                    rstd_of(s.b + 2)
                if isinstance(s.t, int) and s.t == V_FIRST - 1:
                    over_rows(vst[:, 2:3], vst[:, 0:1], (v_small, 1), v_root)
                    pool.wait_ge(v_root, 1)
                    nc.gpsimd.tensor_tensor(vst[:, 1:2], vst[:, 2:3], half[:, :], ALU.pow).then_inc(v_all, 1)
                if isinstance(s.t, int) and s.t < len(V_TILES) - 1:
                    for j in range(V_TILES[s.t], V_TILES[s.t + 1]):
                        if by_pool(j):
                            pool.wait_ge(v_hi, j + 1)
                            nc.gpsimd.tensor_scalar(v_stage(j), v_stage(j), vst[:, 4:5], None, ALU.mult)\
                                .then_inc(v_scaled, 1)
                            pool.wait_ge(v_scaled, j // 4)
                            nc.gpsimd.tensor_tensor(v_pair(j, 1), v_stage(j), v_pair(j, 0), ALU.subtract)\
                                .then_inc(v_ready2, 1)
                if s.c == 2 and s.has_out:
                    wait(pool, x2_in, 16 * (s.b - 1))
                    nc.gpsimd.tensor_tensor(xr[:, :], xr[:, :], obias[:, :], ALU.add).then_inc(xr_ready, 1)

            run(pool, step)

        @block.tensor
        def _(pe):
            def split_product(ps, lhs, rhs, start, stop):
                nc.tensor.matmul(ps, lhs[0], rhs[0], start=start, stop=False)
                nc.tensor.matmul(ps, lhs[0], rhs[1], start=False, stop=False)
                return nc.tensor.matmul(ps, lhs[1], rhs[0], start=False, stop=stop)

            def transpose_x(n):
                wait(pe, xn_ready, n)
                wait(pe, q_ready, n - 1)
                for s in range(ND):
                    last = nc.tensor.transpose(blk(M0, s), blk(xq, s), ident[:, :])
                last.then_inc(xT_done, 1)

            def project_q(n, out_before):
                wait(pe, hT_ready, n)
                for h in range(2):
                    for s in range(ND):
                        nc.tensor.matmul(M0[:, 0:2], ho[:, h, s, :], wpair[:, s, :],
                                         start=(h == 0 and s == 0), stop=(h == 1 and s == ND - 1))
                wait(pe, res_ready, out_before)
                for s in range(ND):
                    last = split_product(M1[:, :], [ho[:, h, s, :] for h in range(2)],
                                         [A_sb[:, h, s, :] for h in range(2)], s == 0, s == ND - 1)
                last.then_inc(qp_done, 1)

            def transpose_q(n):
                wait(pe, q_scaled, n)
                for s in range(ND):
                    last = nc.tensor.transpose(blk(M0, s), blk(xq, s), ident[:, :])
                last.then_inc(qTp_done, 1)

            fill = 0

            def bank_of_next():
                before = last_in_bank(fill)
                if before is not None:
                    by_act = read_by_act(before)
                    pe.wait_ge(start_act if by_act else start_dve, reads(before, by_act))
                elif fill in ASIDE:
                    pe.wait_ge(aside_read, 2)
                return bank_of(fill)

            def filled(last):
                nonlocal fill
                last.then_inc(start_mm, 1)
                fill += 1

            for k in range(ND):
                pe.wait_ge(w_in[k], 32)
                for s in range(ND):
                    last = nc.tensor.matmul(START[s][:, :], Wq_sb[:, k, s * P:(s + 1) * P], Wk_sb[:, k, :],
                                            start=(k == 0), stop=(k == ND - 1))
                    if k == ND - 1:
                        filled(last)
            pe.wait_ge(reps_ready, 1)
            for k in range(ND):
                last = nc.tensor.matmul(S[0][:, :], bqrep[:, k, :], Wk_sb[:, k, :], start=(k == 0), stop=(k == ND - 1))
            last.then_inc(aside_mm, 1)
            for s in range(ND + 1):
                for k in range(ND):
                    lhs = Wq_sb[:, k, s * P:(s + 1) * P] if s < ND else bqrep[:, k, :]
                    last = nc.tensor.matmul(S[1][:, s:s + 1], lhs, bkc[:, k:k + 1], start=(k == 0), stop=(k == ND - 1))
            last.then_inc(aside_mm, 1)
            pe.wait_ge(ident_ready, 2)
            transpose_x(1)
            pe.wait_ge(m_in, 16)
            wmv = Wm_sb.rearrange("f s (e k) -> f s k e", k=ND)
            for k in range(ND):
                ps = bank_of_next()
                for s in range(ND):
                    last = nc.tensor.transpose(blk(ps, s), wmv[:, s, k, :], ident[:, :])
                filled(last)
            pe.wait_ge(start_dve, ND)
            pe.wait_ge(w_ready, 1)
            project_q(1, 0)
            pe.wait_ge(wv_in, 16)

            def product_b(s):
                ps = bank_of_next()
                if s == 0:
                    pe.wait_ge(start_act, ND)
                for k in range(ND):
                    last = nc.tensor.matmul(ps[:, :], Wv_sb[:, k, s * P:(s + 1) * P], WmT[:, k, :],
                                            start=(k == 0), stop=(k == ND - 1))
                filled(last)

            def transpose_key(g):
                pe.wait_ge(k_in[g], 16)
                for s in range(ND):
                    ps = bank_of_next()
                    for m in range(CM):
                        last = nc.tensor.transpose(blk(ps, m), k_stage(g)[:, m, s * P:(s + 1) * P], ident[:, :])
                    filled(last)

            for s in range(ND - 2):
                product_b(s)
            transpose_q(1)
            product_b(ND - 2)
            transpose_key(0)
            product_b(ND - 1)
            transpose_key(1)
            ps = bank_of_next()
            for k in range(ND):
                last = nc.tensor.matmul(ps[:, :], bvrep[:, k, :], WmT[:, k, :], start=(k == 0), stop=(k == ND - 1))
            filled(last)

            def step(s):
                if s.has_scores:
                    if s.c == 0:
                        wait(pe, q_ready, s.b + 1)
                    if isinstance(s.t, int) and s.t < NC:
                        n = last_fill(s.t)
                        if s.t < len(ASIDE):
                            n = max(n, sorted(ASIDE)[s.t])
                        pe.wait_ge(start_dve, reads(n, False))
                    wait(pe, z1_ready, s.t - 1)
                    for f in range(ND):
                        last = split_product(S[s.j % 2][:, :], [qT[:, s.p, h, f, :] for h in range(2)],
                                             [k_pair(s.c, h, f) for h in range(2)], f == 0, f == ND - 1)
                    last.then_inc(scores_done, 1)
                if isinstance(s.t, int) and s.t < NC - FIRST_KEYS:
                    transpose_key(s.t + FIRST_KEYS)
                if s.has_T:
                    ju = s.j - LAG_T
                    if ju % 2 == 0:
                        wait(pe, exp_done, s.pair + 1)
                    wait(pe, p_lo, s.t - LAG_T - 1)
                    probs = Zbuf[:, (ju // NC) % 2, (ju % NC) * CW:(ju % NC + 1) * CW]
                    for m in range(CM):
                        last = nc.tensor.transpose(blk(T[ju % 2], m), blk(probs, m), ident[:, :])
                    last.then_inc(pT_done, 1)
                if s.has_V:
                    jw = s.j - LAG_V
                    wait(pe, p_lo, s.t - LAG_V + 1)
                    if jw % NC == 0:
                        wait(pe, osb_ready, s.b - 2)
                    if isinstance(s.t, int) and s.t < LAG_V + NC:
                        for m in range(CM):
                            in_pairs(pe, (s.t - LAG_V) * CM + m)
                    for m in range(CM):
                        tile = (jw % NC) * CM + m
                        last = split_product(O[(jw // NC) % 2][:, :], [pT[:, jw % 2, h, m, :] for h in range(2)],
                                             [v_pair(tile, h) for h in range(2)],
                                             jw % NC == 0 and m == 0, jw % NC == NC - 1 and m == CM - 1)
                    last.then_inc(pv_done, 1)
                if s.c == 2 and s.has_prep:
                    transpose_x(s.b + 2)
                if s.c == 3 and s.has_prep:
                    project_q(s.b + 2, s.b - 2)
                if s.c == 4 and s.has_out:
                    o = s.b - 2
                    wait(pe, osb_ready, o + 1)
                    if s.has_prep:
                        wait(pe, q_small, Q_SMALL * (s.b + 1) + 1)
                    wait(pe, res_ready, o)
                    for f in range(ND):
                        last = nc.tensor.transpose(blk(M1, f), blk(osb, f), ident[:, :])
                    last.then_inc(oTp_done, 1)
                if s.c == 5 and s.has_prep:
                    transpose_q(s.b + 2)
                if s.c == 6 and s.has_out:
                    wait(pe, oT_ready, s.b - 1)
                    for f in range(ND):
                        last = split_product(M1[:, :], [ho[:, h, f, :] for h in range(2)],
                                             [B_sb[:, h, f, :] for h in range(2)], f == 0, f == ND - 1)
                    last.then_inc(outp_done, 1)

            run(pe, step)

        @block.scalar
        def _(act):
            act.dma_start(bqc[:, :], bq.rearrange("(p k) -> p k", k=ND)).then_inc(b_in, 16)
            act.dma_start(bkc[:, :], bk.rearrange("(p k) -> p k", k=ND)).then_inc(b_in, 16)
            act.dma_start(bvc[:, :], bv.rearrange("(p k) -> p k", k=ND)).then_inc(b_in, 16)
            act.dma_start(obias[:, :], bm.partition_broadcast(P)).then_inc(bm_in, 16)

            def h_T(n, out_before):
                wait(act, xT_done, n)
                wait(act, outp_done, out_before)
                nc.scalar.activation(ho[:, 0, :, :].rearrange("p s n -> p (s n)"), M0[:, :], ACT.Relu).then_inc(h_hi, 1)

            def q_high(n, p):
                wait(act, qTp_done, n)
                nc.scalar.activation(qT[:, p, 0, :, :].rearrange("p s n -> p (s n)"), M0[:, :], ACT.Copy).then_inc(q_hi, 1)

            fill = 0

            def high_of(dst, scale):
                nonlocal fill
                act.wait_ge(start_mm, fill + 1)
                nc.scalar.activation(dst, bank_of(fill)[:, :], ACT.Copy, scale=scale).then_inc(start_hi, 1)
                fill += 1

            def key_high(g):
                for s in range(ND):
                    high_of(k_pair(g, 0, s), kst[:, 4:5])

            def square_key(g):
                act.wait_ge(k_in[g], 16)
                if g > 0:
                    act.wait_ge(k_sum, g)
                scrap = Kbuf[:, 0:2048].bitcast(bf16)[:, 0:CM * D]
                nc.scalar.activation(scrap, k_stage(g).rearrange("p j d -> p (j d)"), ACT.Square,
                                     accum_out=ksum[:, g:g + 1]).then_inc(k_sum, 1)

            act.wait_ge(a_small, 5)
            for s in range(ND):
                high_of(A_sb[:, 0, s, :], ast[:, 4:5])
            act.wait_ge(aside_mm, 1)
            nc.scalar.activation(qbias[:, :], S[0][:, :], ACT.Copy).then_inc(aside_read, 1)
            square_key(0)
            act.wait_ge(aside_mm, 2)
            nc.scalar.activation(wcol[:, :], S[1][:, 0:ND + 1], ACT.Copy, scale=1.0 / ROOT).then_inc(aside_read, 1)
            h_T(1, 0)
            for k in range(ND):
                act.wait_ge(start_mm, fill + 1)
                nc.scalar.activation(WmT[:, k, :], bank_of(fill)[:, :], ACT.Copy).then_inc(start_act, 1)
                fill += 1
            for g in range(1, ACT_SQUARES[0]):
                square_key(g)
            act.wait_ge(b_small, 5)
            for s in range(ND - 1):
                high_of(B_sb[:, 0, s, :], bst[:, 4:5])
                if s == 1:
                    q_high(1, 0)
                for g in range(ACT_SQUARES[s], ACT_SQUARES[s + 1]):
                    square_key(g)
            act.wait_ge(k_small, 5)
            key_high(0)
            high_of(B_sb[:, 0, ND - 1, :], bst[:, 4:5])
            key_high(1)
            fill += 1

            def square_value(g):
                j, m = V_PARTS[g]
                act.wait_ge(v_in[g], 16)
                if g > 0:
                    act.wait_ge(v_sum, g)
                else:
                    act.wait_ge(k_sum2, NC - ACT_SQUARES[-1])
                scrap = pT[:, :, :, :, :].rearrange("p a b m n -> p (a b m n)").bitcast(bf16)[:, 0:m * D]
                nc.scalar.activation(scrap, v_stage(j, m), ACT.Square, accum_out=vsum[:, g:g + 1]).then_inc(v_sum, 1)

            def value_high(j):
                if j == 0:
                    act.wait_ge(v_small, 5)
                if j >= 2:
                    in_pairs(act, j - 2)
                nc.scalar.activation(v_pair(j, 0), v_stage(j), ACT.Copy, scale=vst[:, 4:5]).then_inc(v_hi, 1)

            for g in range(V_SQUARES[0]):
                square_value(g)

            def step(s):
                if s.has_T:
                    ju = s.j - LAG_T
                    wait(act, pT_done, s.t - LAG_T + 1)
                    wait(act, pv_done, s.t - LAG_T - 1)
                    nc.scalar.activation(pT[:, ju % 2, 0, :, :].rearrange("p m n -> p (m n)"), T[ju % 2][:, :],
                                         ACT.Copy, scale=PSCALE).then_inc(p_hi, 1)
                if isinstance(s.t, int) and s.t < NC - FIRST_KEYS:
                    key_high(s.t + FIRST_KEYS)
                if s.has_scores:
                    wait(act, z1_ready, s.t + 1)
                    wait(act, cmax_ready, s.t)
                    nc.scalar.activation(drop[:, :], Zbuf[:, s.p, s.c * CW:(s.c + 1) * CW], ACT.Abs).then_inc(abs_ready, 1)
                if s.c % 2 == 0 and s.has_exp:
                    k, pp = s.c // 2, 1 - s.p
                    if k == 0:
                        wait(act, smax_ready, 2 * s.b)
                    at = Zbuf[:, pp, 2 * k * CW:2 * (k + 1) * CW]
                    nc.scalar.activation(at, at, ACT.Exp, bias=smx[:, pp, 1:2], scale=smx[:, pp, 2:3],
                                         accum_out=psums[:, pp, k:k + 1]).then_inc(exp_done, 1)
                if isinstance(s.t, int) and s.t < len(V_TILES) - 1:
                    for j in range(V_TILES[s.t], V_TILES[s.t + 1]):
                        value_high(j)
                if s.c == 2 and s.has_prep:
                    h_T(s.b + 2, s.b - 2)
                if s.c == 4 and s.has_out:
                    wait(act, oTp_done, s.b - 1)
                    if s.has_prep:
                        wait(act, qp_done, s.b + 2)
                    nc.scalar.activation(ho[:, 0, :, :].rearrange("p s n -> p (s n)"), M1[:, :], ACT.Copy).then_inc(oT_hi, 1)
                if s.c == 5 and s.has_prep:
                    q_high(s.b + 2, 1 - s.p)
                if isinstance(s.t, int) and s.t < len(V_SQUARES) - 1:
                    for g in range(V_SQUARES[s.t], V_SQUARES[s.t + 1]):
                        square_value(g)

            run(act, step)

        @block.vector
        def _(dve):
            def row_stats(n):
                wait(dve, x_in, 16 * n)
                nc.vector.bn_stats(bn[:, :], xq[:, :]).then_inc(bn_ready, 1)

            def mean_var():
                nc.vector.bn_aggr(mv[:, :], bn[:, :]).then_inc(stats_ready, 1)

            def normalise(n):
                wait(dve, rstd_ready, n)
                nc.vector.tensor_scalar(xq[:, :], xq[:, :], mv[:, 0:1], rstd[:, 2:3], ALU.subtract, ALU.mult)\
                    .then_inc(xn_ready, 1)

            def row_scales(n):
                first = Q_SMALL * (n - 1)
                wait(dve, qp_done, n)
                nc.vector.scalar_tensor_tensor(out=xq[:, :], in0=M1[:, :], scalar=ast[:, 5:6], in1=qbias[:, :],
                                               op0=ALU.mult, op1=ALU.add).then_inc(q_small, 1)
                wait(dve, q_small, first + 1)
                nc.vector.tensor_reduce(qst[:, 0:1], xq[:, :], X, ALU.max, apply_absolute_value=True).then_inc(q_small, 1)
                nc.vector.tensor_reduce(qst[:, 4:5], M0[:, 0:2], X, ALU.add).then_inc(q_small, 1)
                wait(dve, q_small, first + 2)
                nc.vector.tensor_scalar_max(qst[:, 1:2], qst[:, 0:1], 2.0 ** -20).then_inc(q_small, 1)
                wait(dve, q_small, first + 3)
                nc.vector.tensor_scalar(qst[:, 5:6], qst[:, 4:5], wst[:, 5:6], wcol[:, ND:ND + 1],
                                        ALU.mult, ALU.add).then_inc(q_small, 1)
                wait(dve, q_small, first + 4)
                nc.vector.tensor_scalar(qst[:, 2:3].bitcast(i32), qst[:, 1:2].bitcast(i32), EXPONENT, None,
                                        ALU.bitwise_and).then_inc(q_small, 1)
                wait(dve, q_small, first + 6)
                nc.vector.reciprocal(qst[:, 3:4], qst[:, 2:3]).then_inc(q_small, 1)
                wait(dve, q_small, first + 7)
                nc.vector.tensor_scalar(xq[:, :], xq[:, :], qst[:, 3:4], TOP, ALU.mult, ALU.mult).then_inc(q_scaled, 1)

            def row_units(n, p):
                first = Q_SMALL * (n - 1)
                wait(dve, q_small, first + 7)
                nc.vector.tensor_scalar(unit[:, p:p + 1], qst[:, 2:3], kunit, None, ALU.mult).then_inc(q_small, 1)
                nc.vector.tensor_scalar(rs[:, p, 0:1], qst[:, 3:4], kper, None, ALU.mult).then_inc(q_small, 1)
                wait(dve, q_small, first + 9)
                nc.vector.tensor_scalar(rs[:, p, 3:4], qst[:, 5:6], rs[:, p, 0:1], None, ALU.mult)
                nc.vector.tensor_scalar(rs[:, p, 1:2], rs[:, p, 0:1], 1e-5, None, ALU.mult)
                nc.vector.tensor_scalar(rs[:, p, 2:3], rs[:, p, 0:1], -1e9, None, ALU.mult).then_inc(q_small, 1)

            def h_low(n):
                wait(dve, h_hi, n)
                nc.vector.scalar_tensor_tensor(out=ho[:, 1, :, :].rearrange("p s n -> p (s n)"), in0=M0[:, :], scalar=0.0,
                                               in1=ho[:, 0, :, :].rearrange("p s n -> p (s n)"),
                                               op0=ALU.max, op1=ALU.subtract).then_inc(hT_ready, 1)

            def oT_low(n):
                wait(dve, oT_hi, n)
                nc.vector.tensor_tensor(ho[:, 1, :, :].rearrange("p s n -> p (s n)"), M1[:, :],
                                        ho[:, 0, :, :].rearrange("p s n -> p (s n)"), ALU.subtract).then_inc(oT_ready, 1)

            def q_low(n, p):
                wait(dve, q_hi, n)
                nc.vector.tensor_tensor(qT[:, p, 1, :, :].rearrange("p s n -> p (s n)"), M0[:, :],
                                        qT[:, p, 0, :, :].rearrange("p s n -> p (s n)"), ALU.subtract).then_inc(q_ready, 1)

            kscale, kunit, kper = kst[:, 4:5], kst[:, 5:6], kst[:, 6:7]
    
            dve.wait_ge(b_in, 48)
            dve.wait_ge(ident_ready, 2)
            for k in range(ND):
                nc.vector.tensor_scalar(bqrep[:, k, :], ident[:, :], 0.0, bqc[:, k:k + 1], ALU.mult, ALU.add)
                last = nc.vector.tensor_scalar(bvrep[:, k, :], ident[:, :], 0.0, bvc[:, k:k + 1], ALU.mult, ALU.add)
            last.then_inc(reps_ready, 1)
            row_stats(1)
            dve.wait_ge(bn_ready, 1)
            mean_var()
            normalise(1)

            def scale_of(st, chain, least, top, unit_of):
                nc.vector.tensor_scalar_max(st[:, 0:1], st[:, 1:2], least).then_inc(chain, 1)
                dve.wait_ge(chain, 2)
                nc.vector.tensor_scalar(st[:, 2:3].bitcast(i32), st[:, 0:1].bitcast(i32), EXPONENT, None,
                                        ALU.bitwise_and).then_inc(chain, 1)
                dve.wait_ge(chain, 3)
                nc.vector.reciprocal(st[:, 3:4], st[:, 2:3]).then_inc(chain, 1)
                nc.vector.tensor_scalar(st[:, 5:6], st[:, 2:3], unit_of, None, ALU.mult)
                dve.wait_ge(chain, 4)
                nc.vector.tensor_scalar(st[:, 4:5], st[:, 3:4], top, None, ALU.mult)
                nc.vector.tensor_scalar(st[:, 6:7], st[:, 3:4], 1.0 / unit_of, None, ALU.mult).then_inc(chain, 1)

            fill = 0

            def low_of(high, low, scale):
                nonlocal fill
                dve.wait_ge(start_hi, sum(f not in ("Wm^T", "bias") for f in FILLS[:fill + 1]))
                nc.vector.scalar_tensor_tensor(out=low, in0=bank_of(fill)[:, :], scalar=scale, in1=high,
                                               op0=ALU.mult, op1=ALU.subtract).then_inc(start_dve, 1)
                fill += 1

            def largest(at, weights):
                for n, w in enumerate(weights):
                    last = nc.vector.tensor_reduce(wmax[:, 0, at + n:at + n + 1], w.rearrange("p k d -> p (k d)"), X,
                                                   ALU.max, apply_absolute_value=True)
                last.then_inc(wmax_ready, 1)

            def scale_of_product(st, chain, at, n, unit_of):
                dve.wait_ge(wmax_all, n)
                nc.vector.tensor_tensor(st[:, 1:2], wmax[:, 1, at:at + 1], wmax[:, 1, at + 1:at + 2], ALU.mult)\
                    .then_inc(chain, 1)
                dve.wait_ge(chain, 1)
                scale_of(st, chain, 2.0 ** -40, 2 * TOP / D, unit_of)

            for k in range(ND):
                dve.wait_ge(w_in[k], 32)
            largest(0, (Wq_sb, Wk_sb))
            scale_of_product(ast, a_small, 0, 1, D / (2 * TOP) / HS)
            for s in range(ND):
                low_of(A_sb[:, 0, s, :], A_sb[:, 1, s, :], ast[:, 4:5])
            dve.wait_ge(aside_read, 2)
            nc.vector.tensor_reduce(wst[:, 0:1], wcol[:, 0:ND], X, ALU.max, apply_absolute_value=True).then_inc(w_small, 1)
            dve.wait_ge(w_all, 1)
            scale_of(wst, w_small, 2.0 ** -40, TOP, 1.0 / (TOP * HS))
            dve.wait_ge(w_small, 5)
            nc.vector.tensor_scalar(wpair[:, :, 0], wcol[:, 0:ND], wst[:, 4:5], None, ALU.mult).then_inc(w_hi, 1)
            dve.wait_ge(w_hi, 1)
            nc.vector.scalar_tensor_tensor(out=wpair[:, :, 1], in0=wcol[:, 0:ND], scalar=wst[:, 4:5], in1=wpair[:, :, 0],
                                           op0=ALU.mult, op1=ALU.subtract).then_inc(w_ready, 1)
            h_low(1)
            dve.wait_ge(m_in, 16)
            dve.wait_ge(wv_in, 16)
            largest(2, (Wm_sb, Wv_sb))
            scale_of_product(bst, b_small, 2, 2, D / (2 * TOP))
            fill += ND

            def square_key(g):
                dve.wait_ge(k_in[g], 16)
                dve.wait_ge(aside_mm, 2)
                if k2 := g - ACT_SQUARES[-1]:
                    dve.wait_ge(k_sum2, k2)
                rows = k_stage(g).rearrange("p j d -> p (j d)")
                scrap = pT[:, :, :, :, :].rearrange("p a b m n -> p (a b m n)").bitcast(bf16)[:, 0:CM * D]
                nc.vector.tensor_tensor_reduce(out=scrap, in0=rows, in1=rows, scale=1.0, scalar=0.0, op0=ALU.mult,
                                               op1=ALU.add, accum_out=ksum[:, g:g + 1]).then_inc(k_sum2, 1)

            def key_low(g):
                for s in range(ND):
                    low_of(k_pair(g, 0, s), k_pair(g, 1, s), kscale)

            row_scales(1)

            def low_b(s):
                low_of(B_sb[:, 0, s, :], B_sb[:, 1, s, :], bst[:, 4:5])

            for s in range(NC - ACT_SQUARES[-1]):
                square_key(ACT_SQUARES[-1] + s)
                low_b(s)
            q_low(1, 0)
            dve.wait_ge(k_sum, ACT_SQUARES[-1])
            dve.wait_ge(k_sum2, NC - ACT_SQUARES[-1])
            nc.vector.tensor_reduce(kst[:, 0:1], ksum[:, :], X, ALU.max).then_inc(k_small, 1)
            dve.wait_ge(k_all, 1)
            scale_of(kst, k_small, 2.0 ** -40, TOP, 1.0 / (TOP * TOP * ROOT))
            dve.wait_ge(k_small, 5)
            low_b(2)
            key_low(0)
            row_units(1, 0)
            low_b(3)
            key_low(1)
            dve.wait_ge(bm_in, 16)
            dve.wait_ge(start_mm, fill + 1)
            nc.vector.tensor_tensor(obias[:, :], bank_of(fill)[:, :], obias[:, :], ALU.add).then_inc(start_dve, 1)
            fill += 1

            def step(s):
                r = s.p
                z = Zbuf[:, r, s.c * CW:(s.c + 1) * CW]
                if s.has_scores:
                    if s.c == 0:
                        wait(dve, q_small, Q_SMALL * (s.b + 1))
                    wait(dve, scores_done, s.t + 1)
                    wait(dve, adj_in[s.j % ADJ_SLOTS], 16 * (s.adj_n + 1))
                    wait(dve, pT_done, s.t - PASS + 1)
                    wait(dve, drop_ready, s.t)
                    nc.vector.scalar_tensor_tensor(out=z, in0=S[s.j % 2][:, :], scalar=rs[:, r, 3:4],
                                                   in1=adjb[:, s.j % ADJ_SLOTS, :], op0=ALU.add, op1=ALU.mult)\
                        .then_inc(z1_ready, 1)
                if s.has_max:
                    if not s.has_scores:
                        wait(dve, drop_ready, s.t)
                    q, c = (s.j - 1) // NC % 2, (s.j - 1) % NC
                    last = Zbuf[:, q, c * CW:(c + 1) * CW]
                    nc.vector.tensor_tensor_reduce(out=last, in0=drop[:, :], in1=last, scale=1.0, scalar=-3.4e38,
                                                   op0=ALU.add, op1=ALU.max, accum_out=cmx[:, q, c:c + 1])\
                        .then_inc(cmax_ready, 1)
                    if s.c == 0:
                        wait(dve, cmax_ready, s.t)
                        nc.vector.tensor_reduce(smx[:, q, 0:1], cmx[:, q, :], X, ALU.max).then_inc(rowmax_ready, 1)
                        wait(dve, exp_done, NPAIR * (s.b - 2))
                        nc.vector.tensor_copy(smx[:, q, 2:3], unit[:, q:q + 1]).then_inc(smax_ready, 1)
                        wait(dve, rowmax_ready, s.b)
                        nc.vector.tensor_scalar(smx[:, q, 1:2], smx[:, q, 0:1], unit[:, q:q + 1], -1.0,
                                                ALU.mult, ALU.mult).then_inc(smax_ready, 1)
                if s.c == 0 and s.has_prep:
                    row_stats(s.b + 2)
                if s.has_T:
                    ju = s.j - LAG_T
                    wait(dve, p_hi, s.t - LAG_T + 1)
                    nc.vector.scalar_tensor_tensor(out=pT[:, ju % 2, 1, :, :].rearrange("p m n -> p (m n)"),
                                                   in0=T[ju % 2][:, :], scalar=PSCALE,
                                                   in1=pT[:, ju % 2, 0, :, :].rearrange("p m n -> p (m n)"),
                                                   op0=ALU.mult, op1=ALU.subtract).then_inc(p_lo, 1)
                if isinstance(s.t, int) and s.t < NC - FIRST_KEYS:
                    key_low(s.t + FIRST_KEYS)
                if s.has_scores:
                    wait(dve, abs_ready, s.t + 1)
                    if s.c == 0 and s.has_prep:
                        wait(dve, bn_ready, s.b + 2)
                    nc.vector.tensor_scalar(drop[:, :], drop[:, :], rs[:, r, 1:2], rs[:, r, 2:3], ALU.is_lt, ALU.mult)\
                        .then_inc(drop_ready, 1)
                if isinstance(s.t, int) and s.t == V_FIRST:
                    dve.wait_ge(v_all, 1)
                    scale_of(vst, v_small, 2.0 ** -40, 2 * TOP, 1.0 / (2 * TOP))
                    dve.wait_ge(v_small, 5)
                    nc.vector.tensor_tensor(ounit[:, :], vst[:, 5:6], bst[:, 5:6], ALU.mult).then_inc(ounit_ready, 1)
                if isinstance(s.t, int) and s.t < len(V_TILES) - 1:
                    for j in range(V_TILES[s.t], V_TILES[s.t + 1]):
                        if not by_pool(j):
                            dve.wait_ge(v_hi, j + 1)
                            nc.vector.scalar_tensor_tensor(out=v_pair(j, 1), in0=v_stage(j), scalar=vst[:, 4:5],
                                                           in1=v_pair(j, 0), op0=ALU.mult, op1=ALU.subtract)\
                                .then_inc(v_ready, 1)
                if isinstance(s.t, int) and s.t == V_FIRST - 1:
                    dve.wait_ge(v_sum, len(V_PARTS))
                    nc.vector.tensor_reduce(vst[:, 0:1], vsum[:, :], X, ALU.max).then_inc(v_small, 1)
                if s.c == 0 and s.has_prep:
                    mean_var()
                if s.c == 1 and s.has_prep:
                    normalise(s.b + 2)
                if s.c == 1 and s.has_out:
                    o, q = s.b - 2, s.p
                    wait(dve, exp_done, NPAIR * (o + 1))
                    nc.vector.tensor_reduce(rsum[:, 0:1], psums[:, q, :], X, ALU.add).then_inc(rsum_ready, 1)
                    wait(dve, rsum_ready, 2 * o + 1)
                    nc.vector.reciprocal(rsum[:, 1:2], rsum[:, 0:1]).then_inc(rsum_ready, 1)
                    wait(dve, rsum_ready, 2 * o + 2)
                    wait(dve, pv_done, NC * (o + 1))
                    wait(dve, oTp_done, o)
                    nc.vector.tensor_scalar(osb[:, :], O[q][:, :], rsum[:, 1:2], 1.0 / PSCALE, ALU.mult, ALU.mult)\
                        .then_inc(osb_ready, 1)
                if s.c == 2 and s.has_prep:
                    h_low(s.b + 2)
                if s.c == 3 and s.has_prep:
                    row_scales(s.b + 2)
                    row_units(s.b + 2, 1 - s.p)
                if s.c == 4 and s.has_out:
                    oT_low(s.b - 1)
                if s.c == 5 and s.has_prep:
                    q_low(s.b + 2, 1 - s.p)
                if s.c == 6 and s.has_out:
                    wait(dve, outp_done, s.b - 1)
                    wait(dve, xr_ready, s.b - 1)
                    if isinstance(s.t, int):
                        dve.wait_ge(ounit_ready, 1)
                    nc.vector.scalar_tensor_tensor(out=xr[:, :], in0=M1[:, :], scalar=ounit[:, :], in1=xr[:, :],
                                                   op0=ALU.mult, op1=ALU.add).then_inc(res_ready, 1)

            run(dve, step)


_INS = ["x", "adj", "L0_gnn_key", "L0_gnn_value", "L0_gnn_Wq", "L0_gnn_bq", "L0_gnn_Wk", "L0_gnn_bk",
        "L0_gnn_Wv", "L0_gnn_bv", "L0_gnn_Wm", "L0_gnn_bm"]
_OUTS = [((4096, 512), "float32")]


def kernel(**inputs):
    import numpy as _np
    import concourse.bacc as _bacc
    from concourse import mybir as _mybir
    from concourse.bass_utils import run_bass_kernel_spmd as _run

    nc = _bacc.Bacc("TRN2", target_bir_lowering=False, num_devices=1)
    arrays, args = {}, []
    for name in _INS:
        a = _np.ascontiguousarray(inputs[name])
        arrays[f"in_{name}_dram"] = a
        args.append(nc.dram_tensor(f"in_{name}_dram", a.shape, _mybir.dt.from_np(a.dtype), kind="ExternalInput").ap())
    for i, (shape, dtype) in enumerate(_OUTS):
        dt = _mybir.dt.from_np(_np.dtype(dtype))
        args.append(nc.dram_tensor(f"out_{i}_dram", shape, dt, kind="ExternalOutput").ap())
    adjacency_attention(nc, *args)
    r = _run(nc, [arrays], core_ids=[0])
    return r.results[0]["out_0_dram"]
```
